# Optimizing a Trainium2 kernel written in Bass

```python
import numpy as np
import jax
import jax.numpy as jnp

def _softmax(x, axis=-1):
    return jax.nn.softmax(x, axis=axis)

def _gelu(x):
    return jax.nn.gelu(x, approximate=True)

def _silu(x):
    return jax.nn.silu(x)

def _sigmoid(x):
    return jax.nn.sigmoid(x)

def _layernorm(x, axis=-1, eps=1e-05):
    m = jnp.mean(x, axis=axis, keepdims=True)
    v = jnp.var(x, axis=axis, keepdims=True)
    return (x - m) / jnp.sqrt(v + eps)

def _scatter_add(tgt, idx, src, axis=0):
    return tgt.at[idx].add(src)

def _segment_sum(src, seg, n):
    return jax.ops.segment_sum(src, seg, n)
kernel_name = 'mk_gnn_ffn_d1_gnn_r8_6ddf81'

def setup_inputs(seed: int=0):
    np.random.seed(seed)
    _w = jnp.asarray

    def _rec_inputs():
        import jax
        import jax.numpy as jnp
        _gk = jax.random.key(seed)
        x = -0.0002117 + 1 * jax.random.normal(jax.random.fold_in(_gk, 1), (6250, 256), jnp.float32)
        src = jax.random.randint(jax.random.fold_in(_gk, 2), (200000,), 0, 6250, jnp.int32)
        dst = jnp.minimum((6250 * jax.random.uniform(jax.random.fold_in(_gk, 3), (200000,)) ** 2.0).astype(jnp.int32), 49999)
        _o = jnp.argsort(dst, stable=True)
        src = src[_o]
        dst = dst[_o]
        edge_attr_2 = jax.random.uniform(jax.random.fold_in(_gk, 11), (200000, 2), jnp.float32, 0.0, 1)
        return (x, src, dst, edge_attr_2)
    x, src, dst, edge_attr_2 = _rec_inputs()

    def _L0_gnn_setup():
        import jax, jax.numpy as jnp
        import numpy as np
        N_NODES = 12500
        N_EDGES = 200000
        IN_FEATS = 256
        OUT_FEATS = 64
        NUM_HEADS = 4
        key = jax.random.key(seed)
        k_h, k_adj, k_dir, k_wf, k_wr, k_af = jax.random.split(key, 6)
        h = jax.random.normal(k_h, (N_NODES, IN_FEATS), dtype=jnp.float32)
        adj = jax.random.randint(k_adj, (2, N_EDGES), 0, N_NODES, dtype=jnp.int64)
        bit = jax.random.randint(k_dir, (N_EDGES,), 0, 2).astype(jnp.float32)
        direction = jnp.stack([bit, 1.0 - bit], axis=1)
        s_w = float(np.sqrt(6.0 / (IN_FEATS + OUT_FEATS)))
        s_a = float(np.sqrt(6.0 / (NUM_HEADS + OUT_FEATS)))
        W_forward = jax.random.uniform(k_wf, (OUT_FEATS, IN_FEATS), jnp.float32, -s_w, s_w)
        W_reverse = jax.random.uniform(k_wr, (OUT_FEATS, IN_FEATS), jnp.float32, -s_w, s_w)
        attn_forward = jax.random.uniform(k_af, (1, NUM_HEADS, OUT_FEATS), jnp.float32, -s_a, s_a)
        return {'h': h, 'adj': adj, 'direction': direction, 'W_forward': W_forward, 'W_reverse': W_reverse, 'attn_forward': attn_forward}
    _L0_gnn_all = _L0_gnn_setup()
    _L0_gnn_in = {k: v for k, v in _L0_gnn_all.items() if k in ('W_forward', 'W_reverse', 'attn_forward')}
    del _L0_gnn_all

    def _L0_ffn_setup():
        import jax, jax.numpy as jnp
        import numpy as np
        B, N, D = (16, 512, 256)
        NUM_EXPERTS, TOP_K, HEADS = (4, 2, 4)
        N_EDGES = 131072
        LN_EPS = 1e-05

        def _layernorm(x, g, b):
            mu = x.mean(-1, keepdims=True)
            var = ((x - mu) ** 2).mean(-1, keepdims=True)
            return (x - mu) * jax.lax.rsqrt(var + LN_EPS) * g + b

        def _forward(x, edge_index, W_gat, att_src, att_dst, b_gat, ln_gamma, ln_beta, W1, b1, W2, b2):
            Bc, Nc, Dc = x.shape
            M = Bc * Nc
            x_flat = x.reshape(M, Dc)
            h = (x_flat @ W_gat).reshape(M, HEADS, NUM_EXPERTS)
            loops = jnp.arange(M, dtype=edge_index.dtype)
            src = jnp.concatenate([edge_index[0], loops])
            dst = jnp.concatenate([edge_index[1], loops])
            a_src = (h * att_src).sum(-1)
            a_dst = (h * att_dst).sum(-1)
            e = jax.nn.leaky_relu(a_src[src] + a_dst[dst], negative_slope=0.2)
            e_max = jax.ops.segment_max(e, dst, num_segments=M)
            ee = jnp.exp(e - e_max[dst])
            denom = jax.ops.segment_sum(ee, dst, num_segments=M)
            alpha = ee / (denom[dst] + 1e-16)
            msg = h[src] * alpha[:, :, None]
            agg = jax.ops.segment_sum(msg, dst, num_segments=M).reshape(M, HEADS * NUM_EXPERTS) + b_gat
            scores = _layernorm(agg, ln_gamma, ln_beta).reshape(M, HEADS, NUM_EXPERTS).mean(1)
            scores = scores.reshape(Bc, Nc, NUM_EXPERTS)
            topk_s, topk_i = jax.lax.top_k(scores, TOP_K)
            w = jax.nn.softmax(topk_s, axis=-1)
            out = jnp.zeros_like(x)
            for ei in range(NUM_EXPERTS):
                g = jnp.where(topk_i == ei, w, 0.0).sum(-1)
                hh = jax.nn.gelu(x @ W1[ei] + b1[ei], approximate=False)
                out = out + g[..., None] * (hh @ W2[ei] + b2[ei])
            return out
        key = jax.random.key(seed)
        ks = jax.random.split(key, 8)
        s = 0.05
        return {'x': jax.random.normal(ks[0], (B, N, D), jnp.float32), 'W_gat': jax.random.normal(ks[1], (D, HEADS * NUM_EXPERTS), jnp.float32) * s, 'att_src': jax.random.normal(ks[2], (HEADS, NUM_EXPERTS), jnp.float32) * s, 'att_dst': jax.random.normal(ks[3], (HEADS, NUM_EXPERTS), jnp.float32) * s, 'b_gat': jnp.zeros((HEADS * NUM_EXPERTS,), jnp.float32), 'ln_gamma': jnp.ones((HEADS * NUM_EXPERTS,), jnp.float32), 'ln_beta': jnp.zeros((HEADS * NUM_EXPERTS,), jnp.float32), 'W1': jax.random.normal(ks[4], (NUM_EXPERTS, D, 2 * D), jnp.float32) * s, 'b1': jnp.zeros((NUM_EXPERTS, 2 * D), jnp.float32), 'W2': jax.random.normal(ks[5], (NUM_EXPERTS, 2 * D, D), jnp.float32) * s, 'b2': jnp.zeros((NUM_EXPERTS, D), jnp.float32), 'edge_index': jax.random.randint(ks[6], (2, N_EDGES), 0, B * N, jnp.int32)}
    _L0_ffn_all = _L0_ffn_setup()
    _L0_ffn_in = {k: v for k, v in _L0_ffn_all.items() if k in ('W_gat', 'att_src', 'att_dst', 'b_gat', 'ln_gamma', 'ln_beta', 'W1', 'b1', 'W2', 'b2', 'edge_index')}
    del _L0_ffn_all
    return {'x': x, 'src': src, 'dst': dst, 'edge_attr_2': edge_attr_2, 'L0_gnn_W_forward': _L0_gnn_in['W_forward'], 'L0_gnn_W_reverse': _L0_gnn_in['W_reverse'], 'L0_gnn_attn_forward': _L0_gnn_in['attn_forward'], 'L0_ffn_W_gat': _L0_ffn_in['W_gat'], 'L0_ffn_att_src': _L0_ffn_in['att_src'], 'L0_ffn_att_dst': _L0_ffn_in['att_dst'], 'L0_ffn_b_gat': _L0_ffn_in['b_gat'], 'L0_ffn_ln_gamma': _L0_ffn_in['ln_gamma'], 'L0_ffn_ln_beta': _L0_ffn_in['ln_beta'], 'L0_ffn_W1': _L0_ffn_in['W1'], 'L0_ffn_b1': _L0_ffn_in['b1'], 'L0_ffn_W2': _L0_ffn_in['W2'], 'L0_ffn_b2': _L0_ffn_in['b2'], 'L0_ffn_edge_index': _L0_ffn_in['edge_index']}

def reference(x, src, dst, edge_attr_2, L0_gnn_W_forward, L0_gnn_W_reverse, L0_gnn_attn_forward, L0_ffn_W_gat, L0_ffn_att_src, L0_ffn_att_dst, L0_ffn_b_gat, L0_ffn_ln_gamma, L0_ffn_ln_beta, L0_ffn_W1, L0_ffn_b1, L0_ffn_W2, L0_ffn_b2, L0_ffn_edge_index):
    import jax
    import jax.numpy as jnp

    def _L0_gnn_ref(h, adj, direction, W_forward, W_reverse, attn_forward):
        import jax, jax.numpy as jnp
        import numpy as np
        N_NODES = 12500
        N_EDGES = 200000
        IN_FEATS = 256
        OUT_FEATS = 64
        NUM_HEADS = 4
        N = h.shape[0]
        H = attn_forward.shape[1]
        h_fwd = h @ W_forward.T
        h_rev = h @ W_reverse.T
        src, dst = (adj[0], adj[1])
        messages = h_fwd[src] * direction[:, 0:1] + h_rev[src] * direction[:, 1:2]
        scores = jnp.einsum('ef,hf->eh', messages, attn_forward[0])
        scores = jax.nn.leaky_relu(scores, negative_slope=0.2)
        exp_scores = jnp.exp(scores - scores.max(axis=0, keepdims=True))
        sum_exp = jax.ops.segment_sum(exp_scores, dst, num_segments=N)
        norm = exp_scores / (sum_exp[dst] + 1e-10)
        outs = [jax.ops.segment_sum(messages * norm[:, hd:hd + 1], dst, num_segments=N) for hd in range(H)]
        out = jnp.stack(outs, axis=1)
        return out.reshape(N, -1)

    def _L0_ffn_ref(x, W_gat, att_src, att_dst, b_gat, ln_gamma, ln_beta, W1, b1, W2, b2, edge_index):
        import jax, jax.numpy as jnp
        import numpy as np
        B, N, D = (16, 512, 256)
        NUM_EXPERTS, TOP_K, HEADS = (4, 2, 4)
        N_EDGES = 131072
        LN_EPS = 1e-05

        def _layernorm(x, g, b):
            mu = x.mean(-1, keepdims=True)
            var = ((x - mu) ** 2).mean(-1, keepdims=True)
            return (x - mu) * jax.lax.rsqrt(var + LN_EPS) * g + b

        def _forward(x, edge_index, W_gat, att_src, att_dst, b_gat, ln_gamma, ln_beta, W1, b1, W2, b2):
            Bc, Nc, Dc = x.shape
            M = Bc * Nc
            x_flat = x.reshape(M, Dc)
            h = (x_flat @ W_gat).reshape(M, HEADS, NUM_EXPERTS)
            loops = jnp.arange(M, dtype=edge_index.dtype)
            src = jnp.concatenate([edge_index[0], loops])
            dst = jnp.concatenate([edge_index[1], loops])
            a_src = (h * att_src).sum(-1)
            a_dst = (h * att_dst).sum(-1)
            e = jax.nn.leaky_relu(a_src[src] + a_dst[dst], negative_slope=0.2)
            e_max = jax.ops.segment_max(e, dst, num_segments=M)
            ee = jnp.exp(e - e_max[dst])
            denom = jax.ops.segment_sum(ee, dst, num_segments=M)
            alpha = ee / (denom[dst] + 1e-16)
            msg = h[src] * alpha[:, :, None]
            agg = jax.ops.segment_sum(msg, dst, num_segments=M).reshape(M, HEADS * NUM_EXPERTS) + b_gat
            scores = _layernorm(agg, ln_gamma, ln_beta).reshape(M, HEADS, NUM_EXPERTS).mean(1)
            scores = scores.reshape(Bc, Nc, NUM_EXPERTS)
            topk_s, topk_i = jax.lax.top_k(scores, TOP_K)
            w = jax.nn.softmax(topk_s, axis=-1)
            out = jnp.zeros_like(x)
            for ei in range(NUM_EXPERTS):
                g = jnp.where(topk_i == ei, w, 0.0).sum(-1)
                hh = jax.nn.gelu(x @ W1[ei] + b1[ei], approximate=False)
                out = out + g[..., None] * (hh @ W2[ei] + b2[ei])
            return out
        return _forward(x, edge_index, W_gat, att_src, att_dst, b_gat, ln_gamma, ln_beta, W1, b1, W2, b2)
    edge_index = jnp.stack([src, dst])
    x = x + _L0_gnn_ref(_layernorm(x, axis=-1), edge_index, edge_attr_2, L0_gnn_W_forward, L0_gnn_W_reverse, L0_gnn_attn_forward)
    x = x + _L0_ffn_ref(_layernorm(x, axis=-1)[None], L0_ffn_W_gat, L0_ffn_att_src, L0_ffn_att_dst, L0_ffn_b_gat, L0_ffn_ln_gamma, L0_ffn_ln_beta, L0_ffn_W1, L0_ffn_b1, L0_ffn_W2, L0_ffn_b2, L0_ffn_edge_index)[0]
    return x

_drawn_inputs = setup_inputs


def setup_inputs(seed=0):
    import zlib

    import numpy as np

    out = dict(_drawn_inputs(seed))
    spreads = {'L0_ffn_b_gat': (0.0, 0.1),
     'L0_ffn_ln_gamma': (1.0, 0.2),
     'L0_ffn_ln_beta': (0.0, 0.1),
     'L0_ffn_b1': (0.0, 0.1),
     'L0_ffn_b2': (0.0, 0.1)}
    factors = {}
    for name, (base, spread) in spreads.items():
        noise = np.random.default_rng([zlib.crc32(name.encode()), seed]).standard_normal(out[name].shape)
        drawn = base * np.exp(spread * noise) if base else spread * noise
        out[name] = jnp.asarray(drawn.astype(out[name].dtype))
    for name, factor in factors.items():
        out[name] = (out[name] * factor).astype(out[name].dtype)
    return out
```

```python
import concourse.bass as bass
from concourse import mybir
from contextlib import ExitStack


class Steps:

    def __init__(self, eng, sem):
        self.eng, self.sem, self.count, self.made = eng, sem, 0, 0

    def link(self, ins):
        self.count = self.count + 1
        self.made += 1
        ins.then_inc(self.sem, 1)
        self.eng.wait_ge(self.sem, self.count)

    def loop(self, n, per, body, first=0):
        start = self.count
        made = self.made
        with self.eng.Fori(first, n) as k:
            self.count = start + (k - first) * per if first else start + k * per
            body(k)
        assert self.made - made == per, (self.made - made, per)
        self.count = start + (n - first) * per


class Signals:

    def __init__(self, sem):
        self.x_loaded = sem("x_loaded")
        self.weights_loaded = sem("weights_loaded")
        self.src_loaded = sem("src_loaded")
        self.attr_loaded = sem("attr_loaded")
        self.dst_loaded = sem("dst_loaded")
        self.graph2_loaded = sem("graph2_loaded")
        self.iota_made = sem("iota_made")
        self.consts_made = sem("consts_made")
        self.x_pad_zero = sem("x_pad_zero")
        self.dve_step = sem("dve_step")
        self.pe_misc = sem("pe_misc")
        self.act_misc = sem("act_misc")
        self.src_clamped = sem("src_clamped")
        self.std1 = sem("std1")
        self.xn1 = sem("xn1")
        self.xn1_T = sem("xn1_T")
        self.xnT1 = sem("xnT1")
        self.row1 = sem("row1")
        self.row1_out = sem("row1_out")
        self.row1_free = sem("row1_free")
        self.row1_dma = sem("row1_dma")
        self.std2 = sem("std2")
        self.xn2 = sem("xn2")
        self.xn2_T = sem("xn2_T")
        self.xnT2 = sem("xnT2")
        self.row2 = sem("row2")
        self.row2_out = sem("row2_out")
        self.x2T_free = sem("x2T_free")
        self.x2T_dma = sem("x2T_dma")
        self.group_table = sem("group_table")
        self.idx_staged = sem("idx_staged")
        self.message_made = sem("message_made")
        self.message_ready = sem("message_ready")
        self.message_stored = sem("message_stored")
        self.key_copies = sem("key_copies")
        self.keys_used = sem("keys_used")
        self.oh_ready = sem("oh_ready")
        self.ohT_ready = sem("ohT_ready")
        self.snap = sem("snap")
        self.before_ready = sem("before_ready")
        self.before_used = sem("before_used")
        self.run_updated = sem("run_updated")
        self.run_seeded = sem("run_seeded")
        self.hist_oh = sem("hist_oh")
        self.hist_mm = sem("hist_mm")
        self.hist_done = sem("hist_done")
        self.start_ready = sem("start_ready")
        self.places_ready = sem("places_ready")
        self.edges_done = sem("edges_done")
        self.x_again = sem("x_again")
        self.probs = sem("probs")
        self.vals_made = sem("vals_made")
        self.block_oh = sem("block_oh")
        self.block_sum = sem("block_sum")
        self.acc_added = sem("acc_added")
        self.vals_free = sem("vals_free")
        self.pool_step = sem("pool_step")
        self.pool_self = sem("pool_self")
        self.records_done = sem("records_done")
        self.x1_ready = sem("x1_ready")
        self.x1_saved = sem("x1_saved")
        self.table2_ready = sem("table2_ready")
        self.table2_saved = sem("table2_saved")
        self.rec_loaded = sem("rec_loaded")
        self.srcq_ready = sem("srcq_ready")
        self.experts_loaded = sem("experts_loaded")
        self.x2_in0 = sem("x2_in0")
        self.x2_in1 = sem("x2_in1")
        self.x2_used = sem("x2_used")
        self.hid_ready = sem("hid_ready")
        self.gelu_done = sem("gelu_done")
        self.y_ready = sem("y_ready")
        self.y_out = sem("y_out")
        self.y_stored = sem("y_stored")
        self.rows_gathered = sem("rows_gathered")
        self.sums_ready = sem("sums_ready")
        self.sums_saved = sem("sums_saved")
        self.ends_ready = sem("ends_ready")
        self.mix_y0 = sem("mix_y0")
        self.mix_y1 = sem("mix_y1")
        self.mixed = sem("mixed")
        self.mix_free = sem("mix_free")
        self.out_dma = sem("out_dma")
        self.out_all = sem("out_all")
        self.msg_dma0 = sem("msg_dma0")
        self.msg_dma1 = sem("msg_dma1")
        self.gath0 = sem("gath0")
        self.gath1 = sem("gath1")
        self.scat0 = sem("scat0")
        self.scat1 = sem("scat1")
        self.msg_in0 = sem("msg_in0")
        self.msg_in1 = sem("msg_in1")
        self.q_dma0 = sem("q_dma0")
        self.q_dma1 = sem("q_dma1")
        self.end_dma = sem("end_dma")
        self.y_dma = sem("y_dma")
        self.pe_soft = sem("pe_soft")
        self.act_soft = sem("act_soft")


def carve(tensor, at, shape, dtype, parts=128):
    n = 1
    for s in shape:
        n *= s
    words = n if dtype != mybir.dt.bfloat16 else (n + 1) // 2
    v = tensor[0:parts, at:at + words]
    if dtype != mybir.dt.float32:
        v = v.bitcast(dtype)
    if len(shape) == 2:
        v = v.rearrange("p (a b) -> p a b", b=shape[1])
    if len(shape) == 3:
        v = v.rearrange("p (a b c) -> p a b c", b=shape[1], c=shape[2])
    return v


def gnn_ffn_kernel(nc, x, src, dst, edge_attr, W_fwd, W_rev, attn, W_gat, att_src, att_dst,
                   b_gat, ln_gamma, ln_beta, W1, b1, W2, b2, edge_index, out):
    f32, i32, bf16 = mybir.dt.float32, mybir.dt.int32, mybir.dt.bfloat16
    ALU, ACT, AX = mybir.AluOpType, mybir.ActivationFunctionType, mybir.AxisListType
    P = 128
    N, D = x.shape
    NB = (N + P - 1) // P
    NP = NB * P
    NPAIR = NB // 2
    assert NB % 2 == 1
    LASTROWS = N - (NB - 1) * P
    H, F = attn.shape[1], attn.shape[2]
    KC = D // P
    EPS = 1e-5
    E1 = src.shape[0]
    EP, EJ = 125, 8
    NG = E1 // (EP * EJ)
    assert NG * EP * EJ == E1 and NG % 2 == 0
    ROW = 2 * (F + H)
    MSG = F + H
    VC = H * F + H
    E2 = edge_index.shape[1]
    T2 = E2 // P
    RT = 6
    HT = 8
    HG = 4
    HGROUPS = T2 // HT // HG
    RGROUPS = NG - HGROUPS
    RLEFT = T2 - RGROUPS * RT
    assert HGROUPS % 2 == 0 and RLEFT >= 0 and RLEFT % 2 == 0 and T2 % HT == 0
    NREC = T2 + NB
    DJ = 8
    ITEMS = (NREC + DJ - 1) // DJ
    NT = ITEMS * DJ
    NQ = NT * P
    assert ITEMS % 2 == 1
    START = 8192
    X = W_gat.shape[1] // H
    HX = H * X
    C2 = HX + 2 * H
    AD, AS = HX, HX + H
    NEG = -1.0e38
    FF = W1.shape[2]
    FM = FF // P
    CH = 448
    NCH = NP // CH
    SUB = 112
    assert NCH * CH == NP and NCH % 2 == 0

    table1 = nc.dram_tensor("table1", [NP, ROW], f32).ap()
    msgs = nc.dram_tensor("msgs", [E1, MSG], f32).ap()
    records = nc.dram_tensor("records", [NQ, 1], i32).ap()
    x1_dram = nc.dram_tensor("x1_dram", [NP, D], f32).ap()
    x2T_dram = nc.dram_tensor("x2T_dram", [P, KC, NP], f32).ap()
    table2 = nc.dram_tensor("table2", [NP, C2], f32).ap()
    y_dram = nc.dram_tensor("y_dram", [NP, X * D], f32).ap()
    sums2 = nc.dram_tensor("sums2", [NQ, C2], f32).ap()

    ctx = ExitStack()
    with ctx:
        def sb(name, shape, dt=f32):
            return ctx.enter_context(nc.sbuf_tensor(name, shape, dt))

        def sem(name):
            return ctx.enter_context(nc.semaphore(name))

        ctx.enter_context(nc.allow_non_contiguous_dma(reason="small transposed loads of weights"))

        big = sb("big", [P, NT * C2])
        two = sb("two", [P, 18880])
        xs = carve(big, 0, [NB, D], f32)
        AC0 = NB * D
        acc = carve(big, AC0, [NB * VC], f32)
        acc3 = carve(big, AC0, [NB, VC], f32)
        at = [AC0]

        def above(shape, dt, parts=P):
            n = 1
            for s in shape:
                n *= s
            v = carve(big, at[0], shape, dt, parts)
            at[0] += n if dt != bf16 else (n + 1) // 2
            return v
        src_i = above([(NG + 1) * EJ], i32)
        attr = above([NG * EJ, 2], f32)
        dst2_i = above([T2], i32)
        src2_i = above([T2], i32)
        smax = above([EJ, H], f32)
        R1_AT = at[0]
        rank_in = above([T2], f32)
        rank_before = above([T2], f32)
        lo_i = carve(big, R1_AT, [T2], i32)
        hi_i = carve(big, R1_AT + T2, [T2], i32)
        part0 = above([EJ, MSG], f32)
        part1 = above([EJ, MSG], f32)
        message = [above([EJ, MSG], f32) for _ in range(2)]
        lo_b = above([T2], bf16)
        hi_b = above([T2], bf16)
        assert at[0] <= NT * C2
        at[0] = 0
        rows_e = [above([EJ, ROW], f32) for _ in range(2)]
        lo_f = above([T2], f32)
        hi_f = above([T2], f32)
        key_f = above([T2], f32)
        oh_lo = [above([P], bf16) for _ in range(RT)]
        oh_hi = [above([NB + 1], bf16) for _ in range(RT)]
        oh_loT = [above([P], f32) for _ in range(RT)]
        hsnap = [above([NB], f32) for _ in range(2)]
        hist_lo = [above([HT, P], bf16) for _ in range(2)]
        hist_hi = [above([HT, NB], bf16) for _ in range(2)]
        junk = [above([P], f32) for _ in range(RT)]
        junk2 = [above([NB], f32) for _ in range(RT)]
        assert at[0] <= AC0
        t2 = carve(big, AC0, [NB, C2], f32)
        prod = carve(big, AC0 + NB * C2, [NB, HX], f32)
        rows2 = carve(big, 0, [NT, C2], f32)
        at2 = [0]

        def low(shape, dt, parts=P):
            n = 1
            for s in shape:
                n *= s
            v = carve(two, at2[0], shape, dt, parts)
            at2[0] += n if dt != bf16 else (n + 1) // 2
            return v
        node_id = low([NP], f32)
        dst_i = low([NG, EJ], i32)
        dst_f = low([NG, EJ], f32)
        V_AT = at2[0]
        vals = [low([EJ, VC], f32) for _ in range(2)]
        extremes = carve(two, V_AT, [2, NG], f32)
        msg_in = [low([EJ, MSG], f32) for _ in range(2)]
        onehot = low([EJ, P], f32)
        REC_AT = 16700
        assert at2[0] <= REC_AT
        at2[0] = 0
        w1_sb = low([X, KC, FF], f32)
        w2_sb = low([X, FM, D], f32)
        hidden = [low([FM, CH], f32) for _ in range(2)]
        x2T = [low([KC, CH], f32) for _ in range(2)]
        y_sb = [low([2, D], f32) for _ in range(2)]
        b2_sb = low([X, D], f32)
        assert at2[0] <= REC_AT
        at2[0] = 0
        not_start = low([NT], f32)
        is_start = low([NT], f32)
        start_neg = low([NT], f32)
        scratch = low([NT], f32)
        decay = [low([NT], f32) for _ in range(H)]
        ends = low([NB, C2], f32)
        agg = low([NB, HX], f32)
        agg2 = low([NB, HX], f32)
        cmp1 = low([NB, X, X], f32)
        cmp2 = low([NB, X, X], f32)
        yblk = [low([X, D], f32) for _ in range(2)]
        xblk = [low([D], f32) for _ in range(2)]
        oblk = [low([D], f32) for _ in range(2)]
        assert at2[0] <= REC_AT
        at2[0] = REC_AT
        place = low([NT], i32)
        record = low([NT], i32)
        assert at2[0] <= 18880
        at2[0] = REC_AT
        rec_q = low([NT], i32)
        src_q = low([NT], i32)

        iota_p = sb("iota_p", [P, 1])
        ident = sb("ident", [P, P])
        ident_b = sb("ident_b", [P, P], bf16)
        iota_row = sb("iota_row", [P, P])
        earlier = sb("earlier", [P, P])
        later = sb("later", [P, P])
        ones = sb("ones", [P, P])
        zeros_b = sb("zeros_b", [P, P], bf16)
        zeros_f = sb("zeros_f", [P, NB])
        eps_t = sb("eps_t", [P, 1])
        wf_sb = sb("wf_sb", [F, D])
        wr_sb = sb("wr_sb", [F, D])
        att_sb = sb("att_sb", [H, F])
        attT = sb("attT", [F, H])
        w_tab = sb("w_tab", [P, KC, ROW])
        wg_sb = sb("wg_sb", [P, KC, HX])
        asrc = sb("asrc", [P, HX])
        adst = sb("adst", [P, HX])
        bgat = sb("bgat", [P, HX])
        gamma = sb("gamma", [P, HX])
        beta = sb("beta", [P, HX])
        b1T = sb("b1T", [P, X * FM])
        stats = sb("stats", [P, NB, 6])
        mv = sb("mv", [P, NB, 2])
        std = sb("std", [P, NB])
        rstd = sb("rstd", [P, NB])
        xn = [sb(f"xn{i}", [P, D]) for i in range(2)]
        xnT = [sb(f"xnT{i}", [P, KC, P]) for i in range(2)]
        row_sb = [sb(f"row_sb{i}", [P, ROW]) for i in range(2)]
        ext_T = sb("ext_T", [P, 4])
        row_i = sb("row_i", [1, 2 * NG], i32)
        blk_i = sb("blk_i", [1, 2 * NG], i32)
        blk_f = sb("blk_f", [1, 2 * NG])
        extra = sb("extra", [1, NG])
        first_f = sb("first_f", [1, NG + 1])
        first_i = sb("first_i", [1, NG + 1], i32)
        cnt1 = sb("cnt1", [P, NB])
        hist = sb("hist", [P, NB])
        incl = sb("incl", [P, NB])
        seg_start = sb("seg_start", [P, NB])
        start1 = sb("start1", [P, NB])
        end_i = sb("end_i", [P, NB], i32)
        gm_p = sb("gm_p", [P, H])
        gm_h = sb("gm_h", [H, 1])
        gm_d = sb("gm_d", [H, H])
        neg_max = sb("neg_max", [P, H])
        src_stage = sb("src_stage", [P, 2, EJ], i32)
        place_stage = sb("place_stage", [P, 2, DJ], i32)
        rec_stage = sb("rec_stage", [P, 2, DJ], i32)
        rinv = sb("rinv", [P, NB, H])
        q_stage = sb("q_stage", [P, 2, DJ], i32)
        q_rows = sb("q_rows", [P, 2, DJ, C2])
        tails = sb("tails", [P, HX + H])
        decays = sb("decays", [P, HX + H])
        any_ns = sb("any_ns", [P, 1])
        any_nb = sb("any_nb", [P, 1])
        pair_sb = sb("pair_sb", [HX + H, 2 * P])
        car_T = sb("car_T", [HX + H, P + 1])
        carry = sb("carry", [P, HX + H])
        m_carry = sb("m_carry", [P, H])
        end_stage = sb("end_stage", [P, 7], i32)
        end_rows = sb("end_rows", [P, 7, C2])
        small = sb("small", [P, NB])
        small2 = sb("small2", [P, NB])
        score = sb("score", [P, NB, X])
        rank = sb("rank", [P, NB, X])
        gate = sb("gate", [P, NB, X])
        lower = sb("lower", [P, X * X])

        ps = [ctx.enter_context(nc.psum_tensor(f"ps{i}", [P, 512], f32)) for i in range(8)]
        p_T = [ps[i][:, 0:KC * P].rearrange("p (c n) -> p c n", c=KC) for i in (0, 1)]
        p_row = [ps[2], ps[3]]
        p_w = ps[4][:, 0:KC * ROW].rearrange("p (c n) -> p c n", c=KC)
        p_key = [ps[0], ps[1]]
        p_before = ps[2][:, 0:RT * NB].rearrange("p (t b) -> p t b", t=RT)
        p_run = ps[3][:, 0:NB]
        p_hist = ps[4][:, 0:NB]
        p_small = ps[5]
        p_acc = ps[6]
        p_hid = [ps[0], ps[1]]
        p_y = [ps[2], ps[3]]
        p_extra = ps[7]

        s = Signals(sem)
        gath, scat = [s.gath0, s.gath1], [s.scat0, s.scat1]
        msg_dma, msg_ready = [s.msg_dma0, s.msg_dma1], [s.msg_in0, s.msg_in1]
        q_dma, x2_in, mix_in = [s.q_dma0, s.q_dma1], [s.x2_in0, s.x2_in1], [s.mix_y0, s.mix_y1]

        def each_block(eng, body):
            with eng.Fori(0, NPAIR) as k:
                body(2 * k, 0, k)
                body(2 * k + 1, 1, k)
            body(NB - 1, 0, NPAIR)

        block = ctx.enter_context(nc.Block())

        @block.sync
        def _(sp):
            sp.wait_ge(s.x_pad_zero, 1)
            sp.dma_start(xs[:, 0:NB - 1, :], x[0:(NB - 1) * P, :].rearrange("(b p) d -> p b d", p=P)) \
                .then_inc(s.x_loaded, 16)
            sp.dma_start(xs[0:LASTROWS, NB - 1, :], x[(NB - 1) * P:N, :]).then_inc(s.x_loaded, 16)
            for v, w in ((wf_sb[:, :], W_fwd), (wr_sb[:, :], W_rev), (att_sb[:, :], attn[0, :, :]),
                         (wg_sb[:, :, :], W_gat.rearrange("(c k) n -> k c n", k=P)),
                         (asrc[:, :], att_src.rearrange("(o h) e -> o (h e)", o=1).to_broadcast([P, HX])),
                         (adst[:, :], att_dst.rearrange("(o h) e -> o (h e)", o=1).to_broadcast([P, HX])),
                         (bgat[:, :], b_gat.rearrange("(o n) -> o n", o=1).to_broadcast([P, HX])),
                         (gamma[:, :], ln_gamma.rearrange("(o n) -> o n", o=1).to_broadcast([P, HX])),
                         (beta[:, :], ln_beta.rearrange("(o n) -> o n", o=1).to_broadcast([P, HX])),
                         (b1T[:, :], b1.rearrange("e (m p) -> p (e m)", p=P))):
                sp.dma_start(v, w).then_inc(s.weights_loaded, 16)
            sp.dma_start(src_i[0:EP, 0:NG * EJ], src.rearrange("(p t) -> p t", p=EP)).then_inc(s.src_loaded, 16)
            sp.dma_start(attr[0:EP, :, :], edge_attr.rearrange("(p t) c -> p t c", p=EP)) \
                .then_inc(s.attr_loaded, 16)
            sp.dma_start(dst2_i, edge_index[1, :].rearrange("(p t) -> p t", p=P)).then_inc(s.graph2_loaded, 16)
            sp.dma_start(src2_i, edge_index[0, :].rearrange("(p t) -> p t", p=P)).then_inc(s.graph2_loaded, 16)
            sp.dma_start(dst_i[0:EP, :, :], dst.rearrange("(g p j) -> p g j", p=EP, j=EJ)) \
                .then_inc(s.dst_loaded, 16)

            sp.sem_inc(s.row1_free, 2)

            def store_row(i, h, k):
                sp.wait_ge(s.row1_out, i + 1 + 2)
                sp.dma_start(table1[bass.ds(i * P, P), :], row_sb[h][:, :]).then_inc(s.row1_dma, 16)
                sp.wait_ge(s.row1_dma, (i + 1) * 16)
                sp.sem_inc(s.row1_free, 1)
            each_block(sp, store_row)

            sp.sem_inc(s.message_stored, 2)
            msg_pt = msgs.rearrange("(p t) c -> p (t c)", p=EP)
            with sp.Fori(0, NG // 2) as k:
                for h in range(2):
                    g = 2 * k + h
                    sp.wait_ge(s.message_ready, g + 1)
                    sp.dma_start(msg_pt[:, bass.ds(g * (EJ * MSG), EJ * MSG)],
                                 message[h][0:EP].rearrange("p j c -> p (j c)")).then_inc(msg_dma[h], 16)
                    sp.wait_ge(msg_dma[h], (k + 1) * 16)
                    sp.sem_inc(s.message_stored, 1)

            sp.wait_ge(s.edges_done, 1)
            sp.dma_start(xs[:, 0:NB - 1, :], x[0:(NB - 1) * P, :].rearrange("(b p) d -> p b d", p=P)) \
                .then_inc(s.x_again, 16)
            sp.dma_start(xs[0:LASTROWS, NB - 1, :], x[(NB - 1) * P:N, :]).then_inc(s.x_again, 16)
            msg_g = msgs.rearrange("(g p j) c -> g p (j c)", p=EP, j=EJ)
            with sp.Fori(0, NG // 2) as k:
                for h in range(2):
                    g = 2 * k + h
                    sp.wait_ge(s.vals_made, g + 1)
                    sp.dma_start(msg_in[h][0:EP].rearrange("p j c -> p (j c)"),
                                 msg_g[bass.ds(g, 1), :, :].rearrange("o p c -> (o p) c")) \
                        .then_inc(msg_ready[h], 16)

            sp.wait_ge(s.x1_ready, 1)
            sp.dma_start(x1_dram.rearrange("(b p) d -> p b d", p=P), xs[:, :, :]).then_inc(s.x1_saved, 16)
            sp.dma_start(w1_sb, W1.rearrange("e (c k) f -> k e c f", k=P)).then_inc(s.experts_loaded, 16)
            sp.dma_start(w2_sb, W2.rearrange("e (c k) d -> k e c d", k=P)).then_inc(s.experts_loaded, 16)
            sp.dma_start(b2_sb.rearrange("p e d -> p (e d)"),
                         b2.rearrange("(o e) d -> o (e d)", o=1).to_broadcast([P, X * D])) \
                .then_inc(s.experts_loaded, 16)
            sp.sem_inc(s.x2T_free, 2)

            def store_x2T(i, h, k):
                sp.wait_ge(s.xnT2, i + 1 + 2)
                sp.dma_start(x2T_dram[:, :, bass.ds(i * P, P)], xnT[h][:, :, :]).then_inc(s.x2T_dma, 16)
                sp.wait_ge(s.x2T_dma, (i + 1) * 16)
                sp.sem_inc(s.x2T_free, 1)
            each_block(sp, store_x2T)
            sp.wait_ge(s.table2_ready, 1)
            sp.dma_start(table2.rearrange("(b p) c -> p b c", p=P), t2[:, :, :]).then_inc(s.table2_saved, 16)
            sp.wait_ge(s.records_done, 1)
            sp.dma_start(rec_q[:, :], records.rearrange("(p t) c -> p (t c)", p=P)).then_inc(s.rec_loaded, 16)

            sp.sem_inc(s.y_stored, 2)

            def load_x2(c, h, n):
                sp.dma_start(x2T[h], x2T_dram[:, :, bass.ds(c * CH, CH)]).then_inc(x2_in[h], 16)
            load_x2(0, 0, 0)
            with sp.Fori(0, NCH // 2) as k:
                for h in range(2):
                    c = 2 * k + h
                    sp.wait_ge(s.x2_used, c + 1)
                    nxt = (c + 1) if h == 0 else (2 * k + 2) % NCH
                    load_x2(nxt, 1 - h, 0)
                    for u in range(2 * X):
                        e, half = u // 2, u % 2
                        n = c * (2 * X) + u
                        sp.wait_ge(s.y_out, n + 1 + 2)
                        sp.dma_start(y_dram[bass.ds(c * CH + half * (2 * SUB), 2 * SUB), e * D:(e + 1) * D]
                                     .rearrange("(a p) d -> p a d", p=SUB), y_sb[u % 2][0:SUB]) \
                            .then_inc(s.y_dma, 16)
                        sp.wait_ge(s.y_dma, (n + 1) * 16)
                        sp.sem_inc(s.y_stored, 1)
            sp.wait_ge(x2_in[0], (NCH // 2 + 1) * 16)

            sp.wait_ge(s.sums_ready, 1)
            sp.dma_start(sums2.rearrange("(p t) c -> p (t c)", p=P), big[:, :]).then_inc(s.sums_saved, 16)

            def mix_io(i, h, k):
                sp.wait_ge(s.mixed, i + 1)
                sp.dma_start(yblk[h].rearrange("p e d -> p (e d)"), y_dram[bass.ds(i * P, P), :]) \
                    .then_inc(mix_in[h], 16)
                sp.dma_start(xblk[h], x1_dram[bass.ds(i * P, P), :]).then_inc(mix_in[h], 16)

            def mix_out(i, h, rows=P):
                sp.wait_ge(s.mixed, i + 1 + 2)
                sp.dma_start(out[bass.ds(i * P, rows), :], oblk[h][0:rows]).then_inc(s.out_dma, 16)
                sp.wait_ge(s.out_dma, (i + 1) * 16)
                sp.sem_inc(s.mix_free, 1)
            sp.sem_inc(s.mix_free, 2)
            sp.wait_ge(s.sums_saved, 16)
            sp.wait_ge(s.x1_saved, 16)
            sp.wait_ge(s.ends_ready, 1)
            mix_io(0, 0, 0)
            with sp.Fori(0, NPAIR) as k:
                mix_io(2 * k + 1, 1, k)
                mix_out(2 * k, 0)
                mix_io(2 * k + 2, 0, k)
                mix_out(2 * k + 1, 1)
            mix_out(NB - 1, 0, LASTROWS)
            sp.wait_ge(s.out_dma, NB * 16)

        @block.gpsimd
        def _(pool):
            pool.iota(iota_p[:, :], [[0, 1]], 0, 1, allow_small_or_imprecise_dtypes=True).then_inc(s.iota_made, 1)
            pool.iota(iota_row[:, :], [[1, P]], 0, 0, allow_small_or_imprecise_dtypes=True) \
                .then_inc(s.iota_made, 1)
            pool.iota(node_id, [[1, NP]], 0, 0, allow_small_or_imprecise_dtypes=True).then_inc(s.iota_made, 1)
            pool.iota(record[:, T2:NREC], [[P, NB]], START, 1).then_inc(s.iota_made, 1)
            pool.iota(record[:, NREC:NT], [[0, NT - NREC]], START, 0).then_inc(s.iota_made, 1)
            pool.iota(place[:, NREC:NT], [[P, NT - NREC]], NREC * P, 1).then_inc(s.iota_made, 1)

            pool.wait_ge(s.row1_free, NB + 2)
            with pool.Fori(0, NG // 2) as k:
                for h in range(2):
                    pool.wait_ge(s.idx_staged, 2 * k + h + 1)
                    pool.nop(nofuse=True)
                    for j in range(EJ):
                        pool.indirect_dma_start(rows_e[h][0:EP, j, :], None, table1,
                                                bass.IndirectOffsetOnAxis(ap=src_stage[0:EP, h, j:j + 1], axis=0)) \
                            .then_inc(gath[h], 16)

            pool.wait_ge(s.places_ready, 1)

            def scatter(item, h, first=False, n=None):
                if not first:
                    pool.wait_ge(scat[h], n * (16 * DJ))
                pool.tensor_copy(place_stage[:, h, :], place[:, bass.ds(item * DJ, DJ)])
                pool.tensor_copy(rec_stage[:, h, :], record[:, bass.ds(item * DJ, DJ)]).then_inc(s.pool_step, 1)
                pool.wait_ge(s.pool_step, item + 1)
                pool.nop(nofuse=True)
                for j in range(DJ):
                    pool.indirect_dma_start(records, bass.IndirectOffsetOnAxis(ap=place_stage[:, h, j:j + 1], axis=0),
                                            rec_stage[:, h, j:j + 1], None).then_inc(scat[h], 16)
            scatter(0, 0, first=True)
            scatter(1, 1, first=True)
            with pool.Fori(1, ITEMS // 2) as k:
                scatter(2 * k, 0, n=k)
                scatter(2 * k + 1, 1, n=k)
            scatter(ITEMS - 1, 0, n=ITEMS // 2)
            pool.wait_ge(scat[0], (ITEMS // 2 + 1) * (16 * DJ))
            pool.wait_ge(scat[1], (ITEMS // 2) * (16 * DJ))
            pool.sem_inc(s.records_done, 1)

            pool.wait_ge(s.table2_saved, 16)
            pool.wait_ge(s.srcq_ready, 1)
            pool.wait_ge(s.x1_saved, 16)

            def stage_q(item, h, count):
                pool.tensor_copy(q_stage[:, h, :], src_q[:, bass.ds(item * DJ, DJ)]).then_inc(s.pool_step, 1)
                pool.wait_ge(s.pool_step, count)
                pool.nop(nofuse=True)
                for j in range(DJ):
                    pool.indirect_dma_start(q_rows[:, h, j, :], None, table2,
                                            bass.IndirectOffsetOnAxis(ap=q_stage[:, h, j:j + 1], axis=0)) \
                        .then_inc(q_dma[h], 16)

            def take_q(item, h, n):
                pool.wait_ge(q_dma[h], (n + 1) * (16 * DJ))
                pool.tensor_copy(rows2[:, bass.ds(item * DJ, DJ), :], q_rows[:, h, :, :]).then_inc(s.pool_self, 1)
                pool.wait_ge(s.pool_self, item + 1)

            stage_q(0, 0, ITEMS + 1)
            with pool.Fori(0, ITEMS // 2) as k:
                stage_q(2 * k + 1, 1, 2 * k + (ITEMS + 2))
                take_q(2 * k, 0, k)
                stage_q(2 * k + 2, 0, 2 * k + (ITEMS + 3))
                take_q(2 * k + 1, 1, k)
            take_q(ITEMS - 1, 0, ITEMS // 2)
            pool.sem_inc(s.rows_gathered, 1)

            pool.wait_ge(s.sums_saved, 16)
            with pool.Fori(0, NB // 7) as k:
                pool.tensor_copy(end_stage[:, :], end_i[:, bass.ds(k * 7, 7)]).then_inc(s.pool_step, 1)
                pool.wait_ge(s.pool_step, k + (2 * ITEMS + 1))
                pool.nop(nofuse=True)
                for j in range(7):
                    pool.indirect_dma_start(end_rows[:, j, :], None, sums2,
                                            bass.IndirectOffsetOnAxis(ap=end_stage[:, j:j + 1], axis=0)) \
                        .then_inc(s.end_dma, 16)
                pool.wait_ge(s.end_dma, (k + 1) * (16 * 7))
                pool.tensor_copy(ends[:, bass.ds(k * 7, 7), :], end_rows[:, :, :]).then_inc(s.pool_self, 1)
                pool.wait_ge(s.pool_self, k + (ITEMS + 1))
            pool.sem_inc(s.ends_ready, 1)

        @block.scalar
        def _(act):
            def project(sd, xn_T, xnT_s, row, row_out, free, width, keep, dram_free):
                act.wait_ge(sd[0], sd[1])
                act.activation(std[:, :], mv[:, :, 1], ACT.Sqrt, bias=eps_t[:, 0:1]).then_inc(sd[2], 1)
                act.sem_inc(xnT_s, 2)
                act.sem_inc(row_out, 2)

                def body(i, h, k):
                    act.wait_ge(xn_T, i + 1 + 2)
                    act.wait_ge(row, i + 1)
                    if dram_free is not None:
                        act.wait_ge(dram_free, i + 1)
                    act.activation(xnT[h][:, :, :], p_T[h], ACT.Copy).then_inc(xnT_s, 1)
                    act.wait_ge(row, i + 1 + 2)
                    if free is not None:
                        act.wait_ge(free, i + 1)
                    act.activation(keep(i, h), p_row[h][:, 0:width], ACT.Copy).then_inc(row_out, 1)
                each_block(act, body)

            act.wait_ge(s.pe_misc, 1)
            act.activation(attT[:, :], p_extra[0:F, 0:H], ACT.Copy).then_inc(s.act_misc, 1)
            act.wait_ge(s.pe_misc, 2)
            act.activation(w_tab[:, :, :], p_w, ACT.Copy).then_inc(s.act_misc, 1)
            project((s.dve_step, STATS1, s.std1), s.xn1_T, s.xnT1, s.row1, s.row1_out, s.row1_free, ROW,
                    lambda i, h: row_sb[h][:, :], None)

            act.wait_ge(s.src_clamped, 1)

            def stage_src(g, h):
                act.wait_ge(s.message_made, g + 1)
                act.activation(src_stage[0:EP, h, :], src_i[0:EP, bass.ds(g * EJ, EJ)], ACT.Copy) \
                    .then_inc(s.idx_staged, 1)

            def snapshot(t, par):
                act.wait_ge(s.run_updated, t + RT)
                act.activation(hsnap[par], p_run, ACT.Copy).then_inc(s.snap, 1)
            stage_src(0, 0)
            with act.Fori(0, HGROUPS // 2) as k:
                stage_src(2 * k + 1, 1)
                stage_src(2 * k + 2, 0)
            act.wait_ge(s.run_seeded, 2)
            with act.Fori(0, RGROUPS // 2) as k:
                for h in range(2):
                    stage_src(2 * k + (HGROUPS + 1 + h), 1 - h)
                    for r in range(RT):
                        snapshot(k * (2 * RT) + (h * RT + r), r % 2)
            for r in range(RLEFT):
                snapshot(RGROUPS * RT + r, r % 2)

            act.wait_ge(s.start_ready, 2)
            with act.Fori(0, NG // 2) as k:
                for h in range(2):
                    g = 2 * k + h
                    act.wait_ge(msg_ready[h], (k + 1) * 16)
                    act.wait_ge(s.vals_free, g + 1)
                    for hd in range(H):
                        ins = act.activation(vals[h][0:EP, :, H * F + hd], msg_in[h][0:EP, :, F + hd], ACT.Exp,
                                             bias=neg_max[0:EP, hd:hd + 1])
                    ins.then_inc(s.probs, 1)

            project((s.x1_ready, 2, s.std2), s.xn2_T, s.xnT2, s.row2, s.row2_out, None, HX,
                    lambda i, h: t2[:, i, 0:HX] if isinstance(i, int) else
                    t2[:, bass.ds(i, 1), 0:HX].rearrange("p o c -> p (o c)"), s.x2T_free)

            act.sem_inc(s.gelu_done, 2)
            act.wait_ge(s.experts_loaded, 48)
            with act.Fori(0, NCH) as c:
                for e in range(X):
                    act.wait_ge(s.y_ready, c * (2 * X) + (2 * e + 2))
                    for m in range(FM):
                        n = c * (X * FM) + (e * FM + m)
                        act.wait_ge(s.hid_ready, n + 1)
                        act.activation(hidden[e % 2][:, m, :], p_hid[m % 2][:, 0:CH], ACT.Gelu,
                                       bias=b1T[:, e * FM + m:e * FM + m + 1]).then_inc(s.gelu_done, 1)

            for hd in range(H):
                act.wait_ge(s.pe_soft, SOFT_PE[hd])
                act.activation(decay[hd], decay[hd], ACT.Exp).then_inc(s.act_soft, 1)
                act.activation(rows2[:, :, AD + hd], rows2[:, :, AD + hd], ACT.Exp).then_inc(s.act_soft, 1)
            act.wait_ge(s.pe_soft, SOFT_DEC)
            act.activation(decays[:, HX:HX + H], decays[:, HX:HX + H], ACT.Exp).then_inc(s.act_soft, 1)
            act.wait_ge(s.pe_soft, SOFT_VAR)
            act.activation(small2[:, :], small[:, :], ACT.Sqrt, bias=eps_t[:, 0:1]).then_inc(s.act_soft, 1)
            act.wait_ge(s.pe_soft, SOFT_EXP)
            act.activation(gate[:, :, :], gate[:, :, :], ACT.Exp).then_inc(s.act_soft, 1)

        @block.tensor
        def _(pe):
            pe.wait_ge(s.consts_made, 1)
            pe.wait_ge(s.weights_loaded, 160)
            nc.tensor.transpose(p_extra[0:F, 0:H], att_sb[:, :], ident[0:H, 0:H]).then_inc(s.pe_misc, 1)
            pe.wait_ge(s.act_misc, 1)
            for c in range(KC):
                for n, w in enumerate((wf_sb, wr_sb)):
                    o = n * MSG
                    nc.tensor.transpose(p_w[:, c, o:o + F], w[:, c * P:(c + 1) * P], ident[0:F, 0:F])
                    last = nc.tensor.matmul(p_w[:, c, o + F:o + MSG], w[:, c * P:(c + 1) * P], attT[:, :],
                                            start=True, stop=True)
            last.then_inc(s.pe_misc, 1)

            def project(xn_s, xn_T, xnT_s, row, row_out, weights, width):
                pe.sem_inc(xn_T, 2)
                pe.sem_inc(row, 2)

                def body(i, h, k):
                    pe.wait_ge(xn_s, i + 1)
                    pe.wait_ge(xnT_s, i + 1)
                    for c in range(KC):
                        last = nc.tensor.transpose(p_T[h][:, c, :], xn[h][:, c * P:(c + 1) * P], ident[:, :])
                    last.then_inc(xn_T, 1)
                    pe.wait_ge(xnT_s, i + 1 + 2)
                    pe.wait_ge(row_out, i + 1)
                    for c in range(KC):
                        last = nc.tensor.matmul(p_row[h][:, 0:width], xnT[h][:, c, :], weights[:, c, :],
                                                start=(c == 0), stop=(c == KC - 1))
                    last.then_inc(row, 1)
                each_block(pe, body)
            pe.wait_ge(s.act_misc, 2)
            project(s.xn1, s.xn1_T, s.xnT1, s.row1, s.row1_out, w_tab, ROW)

            pe.wait_ge(s.group_table, 1)
            for c in range(4):
                last = nc.tensor.transpose(p_small[0:NG // 2, c * EP:(c + 1) * EP],
                                           extremes[0:EP, c // 2, (c % 2) * (NG // 2):(c % 2 + 1) * (NG // 2)],
                                           ident[0:EP, 0:EP])
            last.then_inc(s.pe_misc, 1)
            pe.wait_ge(s.group_table, 2)
            for c in range(4):
                last = nc.tensor.matmul(p_extra[0:1, c * (NG // 2):(c + 1) * (NG // 2)], ext_T[0:NG // 2, c:c + 1],
                                        ident[0:NG // 2, 0:NG // 2], start=True, stop=True)
            last.then_inc(s.pe_misc, 1)

            nc.tensor.matmul(p_hist, zeros_b[:, :], ident_b[:, 0:NB], start=True, stop=False)
            pe.sem_inc(s.hist_mm, 2)
            with pe.Fori(0, HGROUPS) as k:
                for r in range(HG):
                    pe.wait_ge(s.hist_oh, k * HG + (r + 1))
                    for j in range(HT):
                        last = nc.tensor.matmul(p_hist, hist_lo[r % 2][:, j, :], hist_hi[r % 2][:, j, :],
                                                start=False, stop=False)
                    last.then_inc(s.hist_mm, 1)
            nc.tensor.matmul(p_hist, zeros_b[:, :], ident_b[:, 0:NB], start=False, stop=True).then_inc(s.hist_done, 1)
            pe.wait_ge(s.start_ready, 1)
            nc.tensor.matmul(p_small[:, 0:NB], later[:, :], cnt1[:, :], start=True, stop=True)
            nc.tensor.matmul(p_small[:, 64:64 + NB], ones[:, :], cnt1[:, :], start=True, stop=True) \
                .then_inc(s.hist_done, 1)
            pe.wait_ge(s.run_seeded, 1)
            nc.tensor.matmul(p_run, ident[:, :], start1[:, :], start=True, stop=True).then_inc(s.run_seeded, 1)

            pe.sem_inc(s.run_updated, RT)

            def key_copy(t, b):
                pe.wait_ge(s.keys_used, t + 1)
                lo = lo_b[:, bass.ds(t, 1)].to_broadcast([P, P])
                nc.tensor.matmul(p_key[b][:, 0:P], lo, ident_b[:, :], start=True, stop=True)
                nc.tensor.matmul(p_key[b][:, P:2 * P], lo, ident_b[:, :], start=True, stop=False)
                nc.tensor.matmul(p_key[b][:, P:2 * P], hi_b[:, bass.ds(t, 1)].to_broadcast([P, P]),
                                 ident_b[:, :], start=False, stop=True).then_inc(s.key_copies, 1)

            def rank_tiles(t0, count):
                key_copy(t0, 0)
                key_copy(t0 + 1, 1)
                pe.wait_ge(s.before_used, t0 + 1)
                for r in range(count):
                    pe.wait_ge(s.ohT_ready, t0 + (r + 1))
                    pe.wait_ge(s.snap, t0 + (r + 1))
                    nc.tensor.matmul(p_before[:, r, :], oh_loT[r], hsnap[r % 2], start=True, stop=True) \
                        .then_inc(s.before_ready, 1)
                    nc.tensor.matmul(p_run, oh_lo[r], oh_hi[r][:, 0:NB], start=False, stop=True,
                                     skip_group_check=True).then_inc(s.run_updated, 1)
                    if r + 2 < count:
                        key_copy(t0 + (r + 2), r % 2)
            with pe.Fori(0, RGROUPS) as k:
                rank_tiles(k * RT, RT)
            for a in range(0, RLEFT, RT):
                rank_tiles(RGROUPS * RT + a, min(RT, RLEFT - a))

            pe.wait_ge(s.edges_done, 1)
            nc.tensor.transpose(p_small[0:H, 0:EP], gm_p[0:EP, :], ident[0:EP, 0:EP]).then_inc(s.pe_misc, 1)
            pe.wait_ge(s.edges_done, 2)
            nc.tensor.matmul(p_small[:, 128:128 + H], ones[0:H, :], gm_d[:, :], start=True, stop=True) \
                .then_inc(s.pe_misc, 1)

            def block_sum(h, it):
                pe.wait_ge(s.block_oh, it + 1)
                pe.wait_ge(s.acc_added, it + 1)
                for j in range(EJ):
                    last = nc.tensor.matmul(p_acc[:, 0:VC], onehot[0:EP, j, :], vals[h][0:EP, j, :],
                                            start=(j == 0), stop=(j == EJ - 1))
                last.then_inc(s.block_sum, 1)
            pe.sem_inc(s.block_sum, NB)
            with pe.Fori(0, NG // 2) as k:
                for h in range(2):
                    g = 2 * k + h
                    lo = pe.value_load(blk_i[0:1, bass.ds(g, 1)], min_val=0, max_val=NB - 1)
                    hi = pe.value_load(blk_i[0:1, bass.ds(g + NG, 1)], min_val=0, max_val=NB - 1)
                    base = pe.value_load(first_i[0:1, bass.ds(g, 1)], min_val=1, max_val=NG * NB + NB)
                    pe.wait_ge(s.vals_made, g + 1 + 2)
                    block_sum(h, base + lo)
                    with pe.If(lo < hi):
                        with pe.Fori(lo + 1, hi + 1) as b:
                            block_sum(h, base + b)

            project(s.xn2, s.xn2_T, s.xnT2, s.row2, s.row2_out, wg_sb, HX)

            pe.sem_inc(s.y_ready, 4)
            pe.wait_ge(s.experts_loaded, 48)

            def hidden_units(c, h, e):
                for m in range(FM):
                    n = c * (X * FM) + (e * FM + m)
                    pe.wait_ge(s.gelu_done, n + 1)
                    for q in range(KC):
                        last = nc.tensor.matmul(p_hid[m % 2][:, 0:CH], w1_sb[:, e, q, m * P:(m + 1) * P],
                                                x2T[h][:, q, :], start=(q == 0), stop=(q == KC - 1))
                    last.then_inc(s.hid_ready, 1)

            def outputs(c, e):
                pe.wait_ge(s.gelu_done, c * (X * FM) + ((e + 1) * FM + 2))
                for half in range(2):
                    u = c * (2 * X) + (2 * e + half)
                    pe.wait_ge(s.y_out, u + 1)
                    for a in range(2):
                        tok = (2 * half + a) * SUB
                        for m in range(FM):
                            last = nc.tensor.matmul(p_y[half][0:SUB, a * D:(a + 1) * D],
                                                    hidden[e % 2][:, m, tok:tok + SUB], w2_sb[:, e, m, :],
                                                    start=(m == 0), stop=(m == FM - 1))
                    last.then_inc(s.y_ready, 1)
            pe.sem_inc(s.x2_used, 1)
            with pe.Fori(0, NCH // 2) as k:
                for h in range(2):
                    c = 2 * k + h
                    pe.wait_ge(x2_in[h], (k + 1) * 16)
                    hidden_units(c, h, 0)
                    for e in range(1, X):
                        hidden_units(c, h, e)
                        outputs(c, e - 1)
                    outputs(c, X - 1)
                    pe.wait_ge(s.y_out, c * (2 * X) + 2 * X)
                    pe.sem_inc(s.x2_used, 1)

            done = 0
            for n, w in enumerate((H, H, HX + H)):
                pe.wait_ge(s.pe_soft, SOFT_ROWS[n][0])
                nc.tensor.transpose(p_small[0:w, 0:P], tails[:, 0:w], ident[:, :])
                nc.tensor.transpose(p_small[0:w, P:2 * P], decays[:, 0:w], ident[:, :]).then_inc(s.pe_misc, 1)
                pe.wait_ge(s.pe_soft, SOFT_ROWS[n][1])
                nc.tensor.transpose(p_small[:, 256:256 + w], car_T[0:w, 0:P], ident[0:w, 0:w]).then_inc(s.pe_misc, 1)

        @block.vector
        def _(dve):
            st = Steps(dve, s.dve_step)
            V = nc.vector
            st.link(V.memset(xs[:, NB - 1, :], 0.0))
            dve.sem_inc(s.x_pad_zero, 1)
            V.memset(zeros_b[:, :], 0.0)
            V.memset(zeros_f[:, :], 0.0)
            V.memset(ones[:, :], 1.0)
            V.memset(eps_t[:, :], EPS)
            V.memset(lower[:, :], 0.0)
            st.link(V.memset(smax, NEG))
            for e in range(1, X):
                V.memset(lower[:, e * X:e * X + e], 1.0)
            dve.wait_ge(s.iota_made, 6)
            V.tensor_scalar(ident[:, :], iota_row[:, :], iota_p[:, 0:1], None, ALU.is_equal)
            V.tensor_scalar(ident_b[:, :], iota_row[:, :], iota_p[:, 0:1], None, ALU.is_equal)
            V.tensor_scalar(earlier[:, :], iota_row[:, :], iota_p[:, 0:1], None, ALU.is_lt)
            V.tensor_scalar(later[:, :], iota_row[:, :], iota_p[:, 0:1], None, ALU.is_gt).then_inc(s.consts_made, 1)
            dve.wait_ge(s.src_loaded, 16)
            V.memset(src_i[:, NG * EJ:(NG + 1) * EJ], 0)
            V.tensor_scalar(src_i[0:EP, 0:NG * EJ], src_i[0:EP, 0:NG * EJ], N - 1, None, ALU.min) \
                .then_inc(s.src_clamped, 1)

            def statistics():
                with dve.Fori(0, NB) as b:
                    V.bn_stats(stats[:, bass.ds(b, 1), :].rearrange("p o c -> p (o c)"),
                               xs[:, bass.ds(b, 1), :].rearrange("p o c -> p (o c)"))
                st.link(V.memset(small[:, 0:1], 0.0))
                V.tensor_tensor(mv[:, :, 0], stats[:, :, 1], stats[:, :, 4], ALU.add)
                V.tensor_tensor(mv[:, :, 1], stats[:, :, 2], stats[:, :, 5], ALU.add)
                st.link(V.tensor_tensor(small[:, :], stats[:, :, 1], stats[:, :, 4], ALU.subtract))
                V.tensor_scalar(mv[:, :, 0], mv[:, :, 0], 0.5, None, ALU.mult)
                V.tensor_scalar(mv[:, :, 1], mv[:, :, 1], 1.0 / D, None, ALU.mult)
                st.link(V.scalar_tensor_tensor(small[:, :], small[:, :], 0.25, small[:, :], ALU.mult, ALU.mult))
                st.link(V.tensor_tensor(mv[:, :, 1], mv[:, :, 1], small[:, :], ALU.add))

            def normalise(sd, xn_s, xn_T):
                dve.wait_ge(sd, 1)
                st.link(V.reciprocal(rstd[:, :], std[:, :]))

                def body(i, h, k):
                    dve.wait_ge(xn_T, i + 1)
                    one = (lambda t: t[:, i, :]) if isinstance(i, int) else \
                        (lambda t: t[:, bass.ds(i, 1), :].rearrange("p o c -> p (o c)"))
                    V.tensor_scalar(xn[h][:, :], one(xs), one(mv)[:, 0:1], rstd[:, bass.ds(i, 1)],
                                    ALU.subtract, ALU.mult).then_inc(xn_s, 1)
                each_block(dve, body)
            dve.wait_ge(s.x_loaded, 32)
            statistics()
            assert st.count == STATS1, st.count
            normalise(s.std1, s.xn1, s.xn1_T)

            dve.wait_ge(s.graph2_loaded, 32)
            dve.wait_ge(s.row1_out, NB + 2)
            st.link(V.tensor_scalar(dst2_i, dst2_i, N, None, ALU.min))
            V.tensor_copy(key_f, dst2_i)
            V.tensor_scalar(lo_i, dst2_i, P - 1, None, ALU.bitwise_and)
            st.link(V.tensor_scalar(hi_i, dst2_i, P.bit_length() - 1, None, ALU.logical_shift_right))
            V.tensor_copy(lo_f, lo_i)
            V.tensor_copy(hi_f, hi_i)
            V.tensor_copy(lo_b, lo_i)
            st.link(V.tensor_scalar(hi_b, hi_i, P, None, ALU.mult))
            dve.wait_ge(s.dst_loaded, 16)
            st.link(V.tensor_scalar(dst_f[0:EP], dst_i[0:EP], N, None, ALU.min))
            V.tensor_reduce(extremes[0:EP, 0, :], dst_f[0:EP], AX.X, ALU.min)
            V.tensor_reduce(extremes[0:EP, 1, :], dst_f[0:EP], AX.X, ALU.max).then_inc(s.group_table, 1)
            dve.wait_ge(s.pe_misc, 3)
            HALF = NG // 2
            V.tensor_reduce(ext_T[0:HALF, 0:2], p_small[0:HALF, 0:2 * EP].rearrange("p (a b) -> p a b", a=2),
                            AX.X, ALU.min)
            V.tensor_reduce(ext_T[0:HALF, 2:4], p_small[0:HALF, 2 * EP:4 * EP].rearrange("p (a b) -> p a b", a=2),
                            AX.X, ALU.max).then_inc(s.group_table, 1)
            dve.wait_ge(s.pe_misc, 4)
            st.link(V.tensor_copy(row_i[:, :], p_extra[0:1, 0:2 * NG]))
            st.link(V.tensor_scalar(blk_i[:, :], row_i[:, :], P.bit_length() - 1, None, ALU.logical_shift_right))
            st.link(V.tensor_copy(blk_f[:, :], blk_i[:, :]))
            st.link(V.tensor_tensor(extra[:, :], blk_f[:, NG:2 * NG], blk_f[:, 0:NG], ALU.subtract))
            V.memset(first_f[:, 0:1], 0.0)
            st.link(V.memset(blk_f[:, :], 1.0))
            st.link(V.tensor_tensor_scan(first_f[:, 1:NG + 1], extra[:, :], blk_f[:, 0:NG], 0.0, ALU.add, ALU.add))
            st.link(V.tensor_copy(blk_f[:, 0:NG], blk_i[:, 0:NG]))
            st.link(V.tensor_tensor(first_f[:, 0:NG], first_f[:, 0:NG], blk_f[:, 0:NG], ALU.subtract))
            st.link(V.tensor_scalar(first_i[:, :], first_f[:, :], float(NB), None, ALU.add))
            dve.sem_inc(s.group_table, 1)

            dve.sem_inc(s.message_made, 2)
            dve.wait_ge(s.attr_loaded, 16)

            def messages(g, h, k):
                dve.wait_ge(gath[h], (k + 1) * (16 * EJ))
                dve.wait_ge(s.message_stored, g + 1)
                d = attr[0:EP, bass.ds(g * EJ, EJ), :]
                V.tensor_tensor(part0[0:EP], rows_e[h][0:EP, :, 0:MSG], d[:, :, 0:1].to_broadcast([EP, EJ, MSG]),
                                ALU.mult)
                V.tensor_tensor(part1[0:EP], rows_e[h][0:EP, :, MSG:ROW], d[:, :, 1:2].to_broadcast([EP, EJ, MSG]),
                                ALU.mult).then_inc(s.message_made, 1)
                dve.wait_ge(s.message_made, g + 1 + 2)
                st.link(V.tensor_tensor(message[h][0:EP], part0[0:EP], part1[0:EP], ALU.add))
                sc = message[h][0:EP, :, F:MSG]
                st.link(V.scalar_tensor_tensor(sc, sc, 0.2, sc, ALU.mult, ALU.max))
                V.tensor_tensor(smax[0:EP], smax[0:EP], sc, ALU.max).then_inc(s.message_ready, 1)

            def histogram(n, b):
                dve.wait_ge(s.hist_mm, n + 1)
                V.tensor_tensor(hist_lo[b], iota_row[:, :].unsqueeze(1).to_broadcast([P, HT, P]),
                                lo_f[:, bass.ds(n * HT, HT)].unsqueeze(2).to_broadcast([P, HT, P]), ALU.is_equal)
                V.tensor_tensor(hist_hi[b], iota_row[:, 0:NB].unsqueeze(1).to_broadcast([P, HT, NB]),
                                hi_f[:, bass.ds(n * HT, HT)].unsqueeze(2).to_broadcast([P, HT, NB]), ALU.is_equal) \
                    .then_inc(s.hist_oh, 1)

            def hist_body(k):
                for h in range(2):
                    messages(2 * k + h, h, k)
                    for r in range(HG):
                        histogram(k * (2 * HG) + (h * HG + r), r % 2)
            st.loop(HGROUPS // 2, 4, hist_body)
            dve.wait_ge(s.hist_done, 1)
            V.tensor_copy(hist[:, :], p_hist)
            V.tensor_scalar(cnt1[:, :], p_hist, 1.0, None, ALU.add).then_inc(s.start_ready, 1)
            dve.wait_ge(s.hist_done, 2)
            st.link(V.tensor_tensor_scan(incl[:, :], p_small[:, 64:64 + NB], zeros_f[:, :], 0.0, ALU.add, ALU.add))
            st.link(V.tensor_tensor(incl[:, :], incl[:, :], p_small[:, 64:64 + NB], ALU.subtract))
            st.link(V.tensor_tensor(seg_start[:, :], incl[:, :], p_small[:, 0:NB], ALU.add))
            V.tensor_copy(place[:, T2:NREC], seg_start[:, :])
            V.tensor_tensor(end_i[:, :], seg_start[:, :], hist[:, :], ALU.add)
            V.tensor_scalar(start1[:, :], seg_start[:, :], 1.0, None, ALU.add).then_inc(s.run_seeded, 1)
            dve.sem_inc(s.keys_used, 2)
            dve.sem_inc(s.before_used, 1)

            def rank_tiles(t0, count):
                dve.wait_ge(s.keys_used, t0 + 2)
                dve.wait_ge(s.before_used, t0 + 1)
                for r in range(count):
                    t = t0 + r
                    col = bass.ds(t, 1)
                    dve.wait_ge(s.run_updated, t + 1)
                    V.tensor_scalar(oh_lo[r], iota_row[:, :], lo_f[:, col], None, ALU.is_equal)
                    V.tensor_scalar(oh_hi[r][:, 0:NB], iota_row[:, 0:NB], hi_f[:, col], None, ALU.is_equal)
                    dve.wait_ge(s.key_copies, t + 1)
                    V.tensor_scalar(oh_loT[r], p_key[r % 2][:, 0:P], iota_p[:, 0:1], None, ALU.is_equal) \
                        .then_inc(s.ohT_ready, 1)
                    V.scalar_tensor_tensor(junk[r], p_key[r % 2][:, P:2 * P], key_f[:, col], earlier[:, :],
                                           ALU.is_equal, ALU.mult, accum_out=rank_in[:, col]) \
                        .then_inc(s.keys_used, 1)
                dve.wait_ge(s.before_ready, t0 + count)
                for r in range(count):
                    t = t0 + r
                    col = bass.ds(t, 1)
                    V.scalar_tensor_tensor(junk2[r], iota_row[:, 0:NB], hi_f[:, col], p_before[:, r, :],
                                           ALU.is_equal, ALU.mult, accum_out=rank_before[:, col]) \
                        .then_inc(s.before_used, 1)

            def rank_body(k):
                for h in range(2):
                    messages(2 * k + (HGROUPS + h), h, k + HGROUPS // 2)
                    rank_tiles(k * (2 * RT) + h * RT, RT)
            st.loop(RGROUPS // 2, 4, rank_body)
            for a in range(0, RLEFT, RT):
                rank_tiles(RGROUPS * RT + a, min(RT, RLEFT - a))
            st.link(V.memset(junk[0], 0.0))
            V.tensor_tensor(place[:, 0:T2], rank_in, rank_before, ALU.add)
            V.tensor_scalar(record[:, 0:T2], src2_i, N - 1, None, ALU.min).then_inc(s.places_ready, 1)
            V.tensor_reduce(gm_p[0:EP, :], smax[0:EP].rearrange("p j h -> p h j"), AX.X, ALU.max)
            dve.wait_ge(s.idx_staged, NG + 1)
            dve.wait_ge(s.snap, T2)
            dve.wait_ge(s.run_updated, T2 + RT)
            dve.wait_ge(s.message_stored, NG + 2)
            st.link(V.memset(xs[:, NB - 1, :], 0.0))
            dve.sem_inc(s.edges_done, 1)

            dve.wait_ge(s.pe_misc, 5)
            st.link(V.tensor_reduce(gm_h[:, :], p_small[0:H, 0:EP], AX.X, ALU.max))
            V.tensor_scalar(gm_d[:, :], ident[0:H, 0:H], gm_h[:, 0:1], None, ALU.mult).then_inc(s.edges_done, 1)
            V.memset(acc, 0.0)
            dve.wait_ge(s.pe_misc, 6)
            V.tensor_scalar(neg_max[:, :], p_small[:, 128:128 + H], -1.0, None, ALU.mult).then_inc(s.start_ready, 1)
            dve.sem_inc(s.vals_free, 2)
            dve.sem_inc(s.vals_made, 2)
            st.link(V.memset(small[:, 0:1], 0.0))
            dve.sem_inc(s.acc_added, NB + 1)
            dve.sem_inc(s.block_oh, NB)

            def make_vals(g, h):
                dve.wait_ge(s.probs, g + 1)
                V.tensor_tensor(vals[h][0:EP, :, 0:H * F].rearrange("p j (h f) -> p j h f", h=H),
                                msg_in[h][0:EP, :, 0:F].unsqueeze(2).to_broadcast([EP, EJ, H, F]),
                                vals[h][0:EP, :, H * F:VC].unsqueeze(3).to_broadcast([EP, EJ, H, F]),
                                ALU.mult).then_inc(s.vals_made, 1)

            def sum_group(g, h, last=False):
                lo = dve.value_load(blk_i[0:1, bass.ds(g, 1)], min_val=0, max_val=NB - 1)
                hi = dve.value_load(blk_i[0:1, bass.ds(g + NG, 1)], min_val=0, max_val=NB - 1)
                base = dve.value_load(first_i[0:1, bass.ds(g, 1)], min_val=1, max_val=NG * NB + NB)

                def one_hot(b):
                    V.tensor_tensor(onehot[0:EP], node_id[0:EP, bass.ds(b * P, P)].unsqueeze(1).to_broadcast([EP, EJ, P]),
                                    dst_f[0:EP, bass.ds(g, 1), :].rearrange("p o j -> p (o j)")
                                    .unsqueeze(2).to_broadcast([EP, EJ, P]), ALU.is_equal).then_inc(s.block_oh, 1)

                def add(b, i):
                    dve.wait_ge(s.block_sum, i + 1)
                    dve.wait_ge(s.acc_added, i + 1)
                    a = acc[:, bass.ds(b * VC, VC)]
                    V.tensor_tensor(a, a, p_acc[:, 0:VC], ALU.add).then_inc(s.acc_added, 1)
                one_hot(lo)
                if not last:
                    make_vals(g + 1, 1 - h)
                add(lo, base + lo)
                with dve.If(lo < hi):
                    with dve.Fori(lo + 1, hi + 1) as b:
                        one_hot(b)
                        add(b, base + b)
                dve.sem_inc(s.vals_free, 1)
            make_vals(0, 0)
            with dve.Fori(0, NG // 2 - 1) as k:
                sum_group(2 * k, 0)
                sum_group(2 * k + 1, 1)
            sum_group(NG - 2, 0)
            sum_group(NG - 1, 1, last=True)
            total = dve.value_load(first_i[0:1, NG:NG + 1], min_val=NG, max_val=NG * NB + NB)
            dve.wait_ge(s.acc_added, total + 1)

            st.link(V.tensor_scalar(rinv[:, :, :], acc3[:, :, H * F:VC], 1e-10, None, ALU.add))
            st.link(V.reciprocal(rinv[:, :, :], rinv[:, :, :]))
            a4 = acc3[:, :, 0:H * F].rearrange("p b (h f) -> p b h f", h=H)
            st.link(V.tensor_tensor(a4, a4, rinv[:, :, :].unsqueeze(3).to_broadcast([P, NB, H, F]), ALU.mult))
            dve.wait_ge(s.x_again, 32)
            st.link(V.tensor_tensor(xs[:, :, :], xs[:, :, :], acc3[:, :, 0:H * F], ALU.add))
            dve.sem_inc(s.x1_ready, 1)
            statistics()
            dve.sem_inc(s.x1_ready, 1)
            normalise(s.std2, s.xn2, s.xn2_T)
            dve.wait_ge(s.row2_out, NB + 2)
            for w, o in ((adst, AD), (asrc, AS)):
                st.link(V.tensor_tensor(prod[:, :, :], t2[:, :, 0:HX], w[:, :].unsqueeze(1).to_broadcast([P, NB, HX]),
                                        ALU.mult))
                st.link(V.tensor_reduce(t2[:, :, o:o + H],
                                        prod[:, :, :].rearrange("p b (h e) -> p b h e", h=H), AX.X, ALU.add))
            dve.sem_inc(s.table2_ready, 1)
            dve.wait_ge(s.rec_loaded, 16)
            st.link(V.tensor_scalar(src_q[:, :], rec_q[:, :], START - 1, None, ALU.bitwise_and))
            dve.sem_inc(s.srcq_ready, 1)

            dve.sem_inc(s.y_out, 2)
            dve.wait_ge(s.experts_loaded, 48)
            with dve.Fori(0, NCH) as c:
                for u in range(2 * X):
                    n = c * (2 * X) + u
                    dve.wait_ge(s.y_ready, n + 1 + 4)
                    dve.wait_ge(s.y_stored, n + 1)
                    V.tensor_tensor(y_sb[u % 2][0:SUB], p_y[u % 2][0:SUB, :].rearrange("p (a d) -> p a d", a=2),
                                    b2_sb[0:SUB, u // 2:u // 2 + 1, :].to_broadcast([SUB, 2, D]), ALU.add) \
                        .then_inc(s.y_out, 1)
            dve.wait_ge(s.y_stored, NCH * 2 * X + 2)
            dve.wait_ge(x2_in[0], (NCH // 2 + 1) * 16)

            dve.wait_ge(s.rows_gathered, 1)
            V.tensor_scalar(not_start, rec_q[:, :], START, None, ALU.is_lt)
            V.tensor_scalar(is_start, rec_q[:, :], START, None, ALU.is_ge)
            st.link(V.tensor_scalar(start_neg, rec_q[:, :], START, NEG, ALU.is_ge, ALU.mult))
            V.tensor_reduce(any_ns[:, :], not_start, AX.X, ALU.min)
            st.link(V.tensor_reduce(any_nb[:, :], start_neg, AX.X, ALU.min))
            soft = [0]

            def tell():
                dve.sem_inc(s.pe_soft, 1)
                soft[0] += 1
                return soft[0]

            def carries(w, n, op0, empty):
                assert tell() == SOFT_ROWS[n][0]
                dve.wait_ge(s.pe_misc, 7 + 2 * n)
                V.tensor_copy(pair_sb[0:w, :], p_small[0:w, 0:2 * P])
                st.link(V.memset(car_T[0:w, 0:1], empty))
                st.link(V.tensor_tensor_scan(car_T[0:w, 1:P + 1], pair_sb[0:w, P:2 * P], pair_sb[0:w, 0:P], empty,
                                             op0, ALU.add if op0 == ALU.mult else ALU.max))
                assert tell() == SOFT_ROWS[n][1]
                dve.wait_ge(s.pe_misc, 8 + 2 * n)
                st.link(V.tensor_copy(carry[:, 0:w], p_small[:, 256:256 + w]))

            def lane(c):
                return rows2[:, :, c]
            for hd in range(H):
                st.link(V.tensor_tensor(lane(AD + hd), lane(AD + hd), is_start, ALU.mult))
                st.link(V.tensor_tensor_scan(scratch, not_start, lane(AD + hd), 0.0, ALU.mult, ALU.add))
                V.tensor_copy(tails[:, hd:hd + 1], scratch[:, NT - 1:NT])
                st.link(V.tensor_copy(decays[:, hd:hd + 1], any_ns[:, :]))
            carries(H, 0, ALU.mult, 0.0)
            for hd in range(H):
                st.link(V.tensor_tensor_scan(scratch, not_start, lane(AD + hd), carry[:, hd:hd + 1],
                                             ALU.mult, ALU.add))
                st.link(V.tensor_tensor(scratch, scratch, lane(AS + hd), ALU.add))
                st.link(V.scalar_tensor_tensor(lane(AD + hd), scratch, 0.2, scratch, ALU.mult, ALU.max))
                st.link(V.tensor_tensor_scan(lane(AS + hd), start_neg, lane(AD + hd), NEG, ALU.add, ALU.max))
                V.tensor_copy(tails[:, hd:hd + 1], rows2[:, NT - 1, AS + hd:AS + hd + 1])
                st.link(V.tensor_copy(decays[:, hd:hd + 1], any_nb[:, :]))
            carries(H, 1, ALU.add, NEG)
            st.link(V.tensor_copy(m_carry[:, :], carry[:, 0:H]))
            for hd in range(H):
                m = lane(AS + hd)
                st.link(V.tensor_tensor_scan(m, start_neg, lane(AD + hd), m_carry[:, hd:hd + 1], ALU.add, ALU.max))
                V.tensor_tensor(decay[hd][:, 1:NT], m[:, 0:NT - 1], m[:, 1:NT], ALU.subtract)
                V.tensor_tensor(decay[hd][:, 0:1], m_carry[:, hd:hd + 1], m[:, 0:1], ALU.subtract)
                st.link(V.tensor_tensor(lane(AD + hd), lane(AD + hd), m, ALU.subtract))
                st.link(V.tensor_scalar(decay[hd], decay[hd], 0.0, None, ALU.min))
                assert tell() == SOFT_PE[hd]
            for hd in range(H):
                st.link(V.tensor_tensor(decays[:, HX + hd:HX + hd + 1], m_carry[:, hd:hd + 1],
                                        rows2[:, NT - 1, AS + hd:AS + hd + 1], ALU.subtract))
            st.link(V.tensor_scalar(decays[:, HX:HX + H], decays[:, HX:HX + H], 0.0, None, ALU.min))
            assert tell() == SOFT_DEC
            for hd in range(H):
                dve.wait_ge(s.act_soft, 2 * hd + 2)
                st.link(V.tensor_tensor(decay[hd], decay[hd], not_start, ALU.mult))
                for e in range(X):
                    c = hd * X + e
                    st.link(V.tensor_tensor(lane(c), lane(c), lane(AD + hd), ALU.mult))
                    st.link(V.tensor_tensor_scan(scratch, decay[hd], lane(c), 0.0, ALU.mult, ALU.add))
                    st.link(V.tensor_copy(tails[:, c:c + 1], scratch[:, NT - 1:NT]))
                st.link(V.tensor_tensor_scan(scratch, decay[hd], lane(AD + hd), 0.0, ALU.mult, ALU.add))
                st.link(V.tensor_copy(tails[:, HX + hd:HX + hd + 1], scratch[:, NT - 1:NT]))
            dve.wait_ge(s.act_soft, 2 * H + 1)
            st.link(V.tensor_scalar(decays[:, HX:HX + H], decays[:, HX:HX + H], any_ns[:, 0:1], None, ALU.mult))
            st.link(V.tensor_copy(decays[:, 0:HX].rearrange("p (h e) -> p h e", h=H),
                                  decays[:, HX:HX + H].unsqueeze(2).to_broadcast([P, H, X])))
            carries(HX + H, 2, ALU.mult, 0.0)
            for c in range(HX + H):
                hd = c // X if c < HX else c - HX
                V.tensor_tensor_scan(lane(c), decay[hd], lane(c), carry[:, c:c + 1], ALU.mult, ALU.add)
            st.link(V.memset(small[:, 0:1], 0.0))
            dve.sem_inc(s.sums_ready, 1)

            dve.wait_ge(s.ends_ready, 1)
            st.link(V.tensor_scalar(rinv[:, :, :], ends[:, :, HX:HX + H], 1e-16, None, ALU.add))
            st.link(V.reciprocal(rinv[:, :, :], rinv[:, :, :]))
            st.link(V.tensor_tensor(agg.rearrange("p b (h e) -> p b h e", h=H),
                                    ends[:, :, 0:HX].rearrange("p b (h e) -> p b h e", h=H),
                                    rinv[:, :, :].unsqueeze(3).to_broadcast([P, NB, H, X]), ALU.mult))

            def row_of(t):
                return t[:, :].unsqueeze(1).to_broadcast([P, NB, HX])

            def col_of(t):
                return t[:, :].unsqueeze(2).to_broadcast([P, NB, HX])
            st.link(V.tensor_tensor(agg, agg, row_of(bgat), ALU.add))
            st.link(V.tensor_reduce(small[:, :], agg, AX.X, ALU.add))
            st.link(V.tensor_scalar(small[:, :], small[:, :], 1.0 / HX, None, ALU.mult))
            st.link(V.tensor_tensor(agg, agg, col_of(small), ALU.subtract))
            st.link(V.tensor_tensor(agg2, agg, agg, ALU.mult))
            st.link(V.tensor_reduce(small[:, :], agg2, AX.X, ALU.add))
            st.link(V.tensor_scalar(small[:, :], small[:, :], 1.0 / HX, None, ALU.mult))
            assert tell() == SOFT_VAR
            dve.wait_ge(s.act_soft, 2 * H + 2)
            st.link(V.reciprocal(small2[:, :], small2[:, :]))
            st.link(V.tensor_tensor(agg, agg, col_of(small2), ALU.mult))
            st.link(V.tensor_tensor(agg, agg, row_of(gamma), ALU.mult))
            st.link(V.tensor_tensor(agg, agg, row_of(beta), ALU.add))
            st.link(V.tensor_reduce(score[:, :, :], agg.rearrange("p b (h e) -> p b e h", h=H), AX.X, ALU.add))
            st.link(V.tensor_scalar(score[:, :, :], score[:, :, :], 1.0 / H, None, ALU.mult))
            mine = score[:, :, :].unsqueeze(3).to_broadcast([P, NB, X, X])
            other = score[:, :, :].unsqueeze(2).to_broadcast([P, NB, X, X])
            V.tensor_tensor(cmp1, other, mine, ALU.is_gt)
            st.link(V.tensor_tensor(cmp2, other, mine, ALU.is_equal))
            st.link(V.tensor_tensor(cmp2.rearrange("p b e j -> p b (e j)"), cmp2.rearrange("p b e j -> p b (e j)"),
                                    lower[:, :].unsqueeze(1).to_broadcast([P, NB, X * X]), ALU.mult))
            st.link(V.tensor_tensor(cmp1, cmp1, cmp2, ALU.add))
            st.link(V.tensor_reduce(rank[:, :, :], cmp1, AX.X, ALU.add))
            st.link(V.tensor_scalar(rank[:, :, :], rank[:, :, :], 2.0, None, ALU.is_lt))
            st.link(V.tensor_reduce(small[:, :], score[:, :, :], AX.X, ALU.max))
            st.link(V.tensor_tensor(gate[:, :, :], score[:, :, :], small[:, :].unsqueeze(2).to_broadcast([P, NB, X]),
                                    ALU.subtract))
            assert tell() == SOFT_EXP
            dve.wait_ge(s.act_soft, 2 * H + 3)
            st.link(V.tensor_tensor(gate[:, :, :], gate[:, :, :], rank[:, :, :], ALU.mult))
            st.link(V.tensor_reduce(small[:, :], gate[:, :, :], AX.X, ALU.add))
            st.link(V.reciprocal(small[:, :], small[:, :]))
            st.link(V.tensor_tensor(gate[:, :, :], gate[:, :, :], small[:, :].unsqueeze(2).to_broadcast([P, NB, X]),
                                    ALU.mult))
            dve.sem_inc(s.mixed, 2)

            def mix(i, h, k):
                dve.wait_ge(mix_in[h], (k + 1) * 32)
                dve.wait_ge(s.mix_free, i + 1)
                g = gate[:, i, :] if isinstance(i, int) else \
                    gate[:, bass.ds(i, 1), :].rearrange("p o e -> p (o e)")
                a, b = xblk[h], oblk[h]
                for e in range(X):
                    ins = V.scalar_tensor_tensor(b, yblk[h][:, e, :], g[:, e:e + 1], a, ALU.mult, ALU.add)
                    a, b = b, a
                    if e < X - 1:
                        st.link(ins)
                st.link(ins)
                V.tensor_copy(oblk[h], xblk[h]).then_inc(s.mixed, 1)
            start = st.count
            with dve.Fori(0, NPAIR) as k:
                st.count = start + k * (2 * X)
                mix(2 * k, 0, k)
                mix(2 * k + 1, 1, k)
            st.count = start + NPAIR * 2 * X
            mix(NB - 1, 0, NPAIR)


STATS1 = 6
SOFT_ROWS = ((1, 2), (3, 4), (10, 11))
SOFT_PE = (5, 6, 7, 8)
SOFT_DEC = 9
SOFT_VAR = 12
SOFT_EXP = 13

_INS = ['x', 'src', 'dst', 'edge_attr_2', 'L0_gnn_W_forward', 'L0_gnn_W_reverse', 'L0_gnn_attn_forward',
        'L0_ffn_W_gat', 'L0_ffn_att_src', 'L0_ffn_att_dst', 'L0_ffn_b_gat', 'L0_ffn_ln_gamma', 'L0_ffn_ln_beta',
        'L0_ffn_W1', 'L0_ffn_b1', 'L0_ffn_W2', 'L0_ffn_b2', 'L0_ffn_edge_index']
_OUTS = [((6250, 256), 'float32')]


def kernel(**inputs):
    import numpy as _np
    import concourse.bacc as _bacc
    from concourse import mybir as _mybir
    from concourse.bass_utils import run_bass_kernel_spmd as _run

    nc = _bacc.Bacc("TRN2", target_bir_lowering=False, num_devices=1)
    arrays, args = {}, []
    for name in _INS:
        a = _np.ascontiguousarray(inputs[name])
        arrays[f"in_{name}_dram"] = a
        args.append(nc.dram_tensor(f"in_{name}_dram", a.shape, _mybir.dt.from_np(a.dtype), kind="ExternalInput").ap())
    for i, (shape, dtype) in enumerate(_OUTS):
        dt = _mybir.dt.from_np(_np.dtype(dtype))
        args.append(nc.dram_tensor(f"out_{i}_dram", shape, dt, kind="ExternalOutput").ap())
    gnn_ffn_kernel(nc, *args)
    r = _run(nc, [arrays], core_ids=[0])
    return r.results[0]["out_0_dram"]
```
